# Optimizing a Trainium2 kernel written in Bass

```python
import numpy as np
import jax
import jax.numpy as jnp

def _softmax(x, axis=-1):
    return jax.nn.softmax(x, axis=axis)
def _gelu(x):
    return jax.nn.gelu(x, approximate=True)
def _silu(x):
    return jax.nn.silu(x)
def _sigmoid(x):
    return jax.nn.sigmoid(x)
def _layernorm(x, axis=-1, eps=1e-5):
    m = jnp.mean(x, axis=axis, keepdims=True)
    v = jnp.var(x, axis=axis, keepdims=True)
    return (x - m) / jnp.sqrt(v + eps)
def _scatter_add(tgt, idx, src, axis=0):
    return tgt.at[idx].add(src)
def _segment_sum(src, seg, n):
    return jax.ops.segment_sum(src, seg, n)

kernel_name = 'mk_conv_seq_d1_conv_nhwc512_d753d5'

def setup_inputs(seed: int = 0):
    np.random.seed(seed)
    _w = jnp.asarray
    def _rec_inputs():
        import jax
        import jax.numpy as jnp
        _gk = jax.random.key(seed)
        x = -9.26e-05 + 0.9999 * jax.random.normal(jax.random.fold_in(_gk, 1), (8, 96, 96, 512), jnp.float32)
        return x
    x = _rec_inputs()
    def _L0_conv_setup():
        import jax, jax.numpy as jnp
        import numpy as np
        NEG_INF = -1e+30

        def _cc_attention(q, k, v):
            B, H, W, _ = q.shape
            sv = jnp.einsum('bhwc,bgwc->bhwg', q, k)
            eye = jnp.eye(H, dtype=bool)[:, None, :]
            sv = jnp.where(eye, NEG_INF, sv)
            sh = jnp.einsum('bhwc,bhuc->bhwu', q, k)
            a = jax.nn.softmax(jnp.concatenate([sv, sh], axis=-1), axis=-1)
            av, ah = (a[..., :H], a[..., H:H + W])
            yv = jnp.einsum('bhwg,bgwc->bhwc', av, v)
            yh = jnp.einsum('bhwu,bhuc->bhwc', ah, v)
            return yv + yh
        key = jax.random.key(seed)
        ks = jax.random.split(key, 7)
        B, H, W, C = (8, 96, 96, 512)
        c = C // 8
        s = lambda n: 1.0 / np.sqrt(n)
        return {'x': jax.random.normal(ks[0], (B, H, W, C), jnp.float32), 'Wq': jax.random.normal(ks[1], (C, c), jnp.float32) * s(C), 'bq': jnp.zeros((c,), jnp.float32), 'Wk': jax.random.normal(ks[2], (C, c), jnp.float32) * s(C), 'bk': jnp.zeros((c,), jnp.float32), 'Wv': jax.random.normal(ks[3], (C, C), jnp.float32) * s(C), 'bv': jnp.zeros((C,), jnp.float32), 'gamma': jnp.float32(0.5)}
    _L0_conv_all = _L0_conv_setup()
    _L0_conv_in = {k: v for k, v in _L0_conv_all.items() if k in ('Wq', 'bq', 'Wk', 'bk', 'Wv', 'bv', 'gamma', )}
    del _L0_conv_all

    return {
        "x": x,
        "L0_conv_Wq": _L0_conv_in["Wq"],
        "L0_conv_bq": _L0_conv_in["bq"],
        "L0_conv_Wk": _L0_conv_in["Wk"],
        "L0_conv_bk": _L0_conv_in["bk"],
        "L0_conv_Wv": _L0_conv_in["Wv"],
        "L0_conv_bv": _L0_conv_in["bv"],
        "L0_conv_gamma": _L0_conv_in["gamma"],
    }

def reference(x, L0_conv_Wq, L0_conv_bq, L0_conv_Wk, L0_conv_bk, L0_conv_Wv, L0_conv_bv, L0_conv_gamma):
    import jax
    import jax.numpy as jnp
    def _L0_conv_ref(x, Wq, bq, Wk, bk, Wv, bv, gamma):
        import jax, jax.numpy as jnp
        import numpy as np
        NEG_INF = -1e+30

        def _cc_attention(q, k, v):
            B, H, W, _ = q.shape
            sv = jnp.einsum('bhwc,bgwc->bhwg', q, k)
            eye = jnp.eye(H, dtype=bool)[:, None, :]
            sv = jnp.where(eye, NEG_INF, sv)
            sh = jnp.einsum('bhwc,bhuc->bhwu', q, k)
            a = jax.nn.softmax(jnp.concatenate([sv, sh], axis=-1), axis=-1)
            av, ah = (a[..., :H], a[..., H:H + W])
            yv = jnp.einsum('bhwg,bgwc->bhwc', av, v)
            yh = jnp.einsum('bhwu,bhuc->bhwc', ah, v)
            return yv + yh
        q = jnp.einsum('bhwc,cd->bhwd', x, Wq) + bq
        k = jnp.einsum('bhwc,cd->bhwd', x, Wk) + bk
        v = jnp.einsum('bhwc,cd->bhwd', x, Wv) + bv
        y = _cc_attention(q, k, v) * gamma
        return y + x

    def _gn(v, G=32, eps=1e-5):
        B_, H_, W_, C_ = v.shape
        g = v.reshape(B_, H_, W_, G, C_ // G)
        m = jnp.mean(g, axis=(1, 2, 4), keepdims=True)
        s = jnp.var(g, axis=(1, 2, 4), keepdims=True)
        return ((g - m) / jnp.sqrt(s + eps)).reshape(v.shape)

    def _ln_c(v, eps=1e-6):
        m = jnp.mean(v, axis=-1, keepdims=True)
        s = jnp.var(v, axis=-1, keepdims=True)
        return (v - m) / jnp.sqrt(s + eps)

    def _ln_t(v, eps=1e-5):
        m = jnp.mean(v, axis=-1, keepdims=True)
        s = jnp.var(v, axis=-1, keepdims=True)
        return (v - m) / jnp.sqrt(s + eps)

    def _to_tokens(v):
        B_, H_, W_, C_ = v.shape
        return v.reshape(B_, H_ * W_, C_)
    def _from_tokens(t, like):
        return t.reshape(like.shape)

    x = _L0_conv_ref(x, L0_conv_Wq, L0_conv_bq, L0_conv_Wk, L0_conv_bk, L0_conv_Wv, L0_conv_bv, L0_conv_gamma)
    return x


_drawn_inputs = setup_inputs


def setup_inputs(seed=0):
    import zlib

    import numpy as np

    out = dict(_drawn_inputs(seed))
    spreads = {'L0_conv_bq': (0.0, 0.1), 'L0_conv_bk': (0.0, 0.1), 'L0_conv_bv': (0.0, 0.1)}
    factors = {}
    for name, (base, spread) in spreads.items():
        noise = np.random.default_rng([zlib.crc32(name.encode()), seed]).standard_normal(out[name].shape)
        drawn = base * np.exp(spread * noise) if base else spread * noise
        out[name] = jnp.asarray(drawn.astype(out[name].dtype))
    for name, factor in factors.items():
        out[name] = (out[name] * factor).astype(out[name].dtype)
    return out
```

```python
import concourse.bass as bass
from concourse import mybir
from contextlib import ExitStack


FP32 = mybir.dt.float32
FP32R = mybir.dt.float32r
ALU = mybir.AluOpType
ACT = mybir.ActivationFunctionType
AX = mybir.AxisListType
NEG_INF = -1e30
WARM = (3, 3, 4, 14, 0, 3, 0)


class At:

    def __init__(self, group, n, pair, buf, known):
        self.g, self.n, self.pair, self.buf, self.known = group, n, pair, buf, known

    def past(self, k):
        return self.known is None or self.known >= k


def pipeline(eng, image, count, steps):
    leads = [lead for lead, _ in steps]
    start = 2 - min(leads)
    start += start % 2
    end = count - max(leads)
    end -= (end - start) % 2

    def turn(t, j):
        for lead, step in steps:
            i = t + lead
            if j is None:
                if 0 <= i < count:
                    step(At(i, image * count + i, image * (count // 2) + i // 2, i % 2, i))
            else:
                step(At(j * 2 + i, image * count + j * 2 + i, image * (count // 2) + j + i // 2, i % 2, None))

    for t in range(-max(leads), start):
        turn(t, None)
    with eng.Fori(0, (end - start) // 2) as j:
        turn(start, j)
        turn(start + 1, j)
    for t in range(end, count - min(leads)):
        turn(t, None)


def criss_cross_attention(nc, x, w_q, b_q, w_k, b_k, w_v_in, b_v, gamma, out):
    B, H, W, C = x.shape
    D = w_q.shape[1]
    P = 128
    assert H == W and 2 * D == P and C % P == 0
    L = W
    KC = C // P
    R = 4
    GR = H // R
    TOK = R * W
    T = TOK // P
    S = 3
    GC = W // S
    HALF = R // 2

    x_tiles = x.rearrange("b (g r) w c -> (b g) (r w) c", r=R).rearrange("n (p t) c -> n p t c", t=T)
    out_tiles = out.rearrange("b (g r) w c -> (b g) (r w) c", r=R).rearrange("n (p t) c -> n p t c", t=T)
    x_rows = x.rearrange("b (g r) w c -> (b g) w r c", r=R)
    x_cols = x.rearrange("b h (g s) c -> b g h s c", s=S)
    e_scratch = nc.dram_tensor("row_exps", (B * GR, W, R * L), FP32, kind="Internal").ap()
    wv_scratch = nc.dram_tensor("wv_parts", (2, P, KC * C), FP32, kind="Internal").ap()

    KIB = 1024
    base = 16512
    mixed_at = base
    kq_at = mixed_at + 4 * KC * H * W
    free_at = kq_at + 4 * H * W

    def at(offset, name, shape, dtype=FP32):
        return nc.alloc_sbuf_tensor_at(name, shape, dtype, offset=offset)

    class Place:

        def __init__(self, offset, end):
            self.offset, self.end = offset, end

        def tensor(self, name, shape, dtype=FP32):
            size = 4
            for n in shape[1:]:
                size *= n
            t = at(self.offset, name, shape, dtype)
            self.offset += (size + 31) // 32 * 32
            assert self.offset <= self.end, (name, self.offset, self.end)
            return t

    end_of_sbuf = 229344
    keep = Place(free_at, end_of_sbuf)
    ident = keep.tensor("ident", [P, P])
    diag = keep.tensor("diag", [L, L])
    bias_out = keep.tensor("bias_out", [P, C])
    bias_kq = keep.tensor("bias_kq", [P, 1])
    gam = keep.tensor("gam", [P, 1])
    w_kq = [keep.tensor(f"w_kq_{part}", [P, KC, P], FP32R) for part in ("hi", "lo")]
    nmax_row = keep.tensor("nmax_row", [W, H])
    sum_row = keep.tensor("sum_row", [W, H])
    nmax_row_t = keep.tensor("nmax_row_t", [H, W])
    sum_row_t = keep.tensor("sum_row_t", [H, W])
    factor = keep.tensor("factor", [H, W])
    factor_t = keep.tensor("factor_t", [W, H])
    free_at = keep.offset
    mixed = at(mixed_at, "mixed", [P, KC, H * W])
    a = Place(mixed_at, kq_at)
    xa = [a.tensor(f"xa{i}", [P, T, C]) for i in range(2)]
    xt_hi = [a.tensor(f"xt_hi{i}", [P, KC, TOK], FP32R) for i in range(2)]
    xt_lo = [a.tensor(f"xt_lo{i}", [P, KC, TOK], FP32R) for i in range(2)]
    q_rows = [a.tensor(f"q_rows{i}", [D, TOK]) for i in range(2)]
    e_rows = [a.tensor(f"e_rows{i}", [W, R, L]) for i in range(2)]
    wv_raw = a.tensor("wv_raw", [P, KC, C])
    w_kq_raw = a.tensor("w_kq_raw", [P, KC, P])
    kq = at(kq_at, "kq", [P, H * W])
    c = Place(kq_at, kq_at + 4 * H * W)
    xr = c.tensor("xr", [W, R, C])
    e_in = [c.tensor(f"e_in{i}", [W, R, L]) for i in range(2)]
    mix_hi = [c.tensor(f"mix_hi{i}", [P, KC, P], FP32R) for i in range(2)]
    mix_lo = [c.tensor(f"mix_lo{i}", [P, KC, P], FP32R) for i in range(2)]
    assert c.offset - kq_at >= 4 * 3 * TOK
    xo = [c.tensor(f"xo{i}", [P, T, C]) for i in range(2)]
    b = Place(free_at, end_of_sbuf)
    xc = [b.tensor("xc0", [H, S, C])]
    q_cols = [b.tensor(f"q_cols{i}", [D, S, H]) for i in range(2)]
    assert b.offset - free_at >= 4 * KC * C
    p_cols = [b.tensor(f"p_cols{i}", [H, S, L]) for i in range(2)]
    pt_cols = b.tensor("pt_cols", [L, S * H])
    small = [[b.tensor(f"{name}{i}", [H, S]) for i in range(2)]
             for name in ("nmax_col", "nmax", "gap", "sum_col", "shrink", "row_part", "total", "inv")]
    nmax_col, nmax, gap, sum_col, shrink, row_part, total, inv = small
    xc.append(b.tensor("xc1", [H, S, C]))
    v = Place(free_at, end_of_sbuf)
    w_v = [v.tensor(f"w_v_{part}", [P, KC, C], FP32R) for part in ("hi", "lo")]
    pt_rows = v.tensor("pt_rows", [L, R * W])

    ctx = ExitStack()
    bank = [ctx.enter_context(nc.psum_tensor(f"bank{i}", [P, 512], FP32)) for i in range(8)]

    def sem(name):
        return ctx.enter_context(nc.semaphore(name))

    def sems(name, n):
        return [sem(f"{name}{i}") for i in range(n)]

    consts_loaded = sem("consts_loaded")
    zeroed = sem("zeroed")
    consts_made = sem("consts_made")
    wv_scaled = sem("wv_scaled")
    bias_scaled = sem("bias_scaled")
    w_hi_made = sem("w_hi_made")
    w_lo_made = sem("w_lo_made")
    stored = sems("stored", 2)
    xa_loaded = sems("xa_loaded", 2)
    xt_made = sems("xt_made", KC)
    xt_hi_made = sems("xt_hi_made", KC)
    xt_lo_made = sems("xt_lo_made", KC)
    kq_made = sem("kq_made")
    kq_kept = sem("kq_kept")
    q_rows_made = sem("q_rows_made")
    row_scores_made = sem("row_scores_made")
    row_max_made = sem("row_max_made")
    row_exps_made = sem("row_exps_made")
    row_exps_kept = sems("row_exps_kept", 2)
    nmax_turned = sem("nmax_turned")
    nmax_t_made = sem("nmax_t_made")
    sum_turned = sem("sum_turned")
    sum_t_made = sem("sum_t_made")
    factor_turned = sem("factor_turned")
    factor_t_made = sem("factor_t_made")
    wv_loaded = sem("wv_loaded")
    xc_loaded = sems("xc_loaded", 2)
    q_cols_made = sem("q_cols_made")
    col_scores_made = sem("col_scores_made")
    col_scores_masked = sem("col_scores_masked")
    col_max_made = sem("col_max_made")
    joint_max_made = sem("joint_max_made")
    gap_made = sem("gap_made")
    shrink_made = sem("shrink_made")
    row_part_made = sem("row_part_made")
    total_made = sem("total_made")
    inv_made = sem("inv_made")
    factor_made = sem("factor_made")
    p_cols_made = sem("p_cols_made")
    p_cols_turned = sem("p_cols_turned")
    pt_cols_made = sem("pt_cols_made")
    col_mixed = sems("col_mixed", S)
    col_kept = sems("col_kept", S)
    xr_loaded = sems("xr_loaded", 2)
    e_in_loaded = sems("e_in_loaded", 2)
    xo_loaded = sems("xo_loaded", 2)
    p_rows_made = sem("p_rows_made")
    p_rows_turned = sem("p_rows_turned")
    pt_rows_made = sem("pt_rows_made")
    row_mixed = sems("row_mixed", R)
    row_added = sems("row_added", R)
    mix_hi_made = sems("mix_hi_made", T)
    mix_lo_made = sems("mix_lo_made", T)
    projected = sems("projected", T)
    xo_biased = sem("xo_biased")
    out_made = sems("out_made", T)

    A_XT, A_KQ, A_S = 0, 4, 6
    B_Z, B_PT, B_S = 0, 4, (3, 5)
    B_NMAX, B_SUM, B_F = 4, 6, 7
    C_Z, C_PT, C_Y = 0, 4, 5

    block = ctx.enter_context(nc.Block())

    @block.sync
    def _(sp):
        for k in range(2):
            src, dst = ((w_k, w_kq_raw[:, :, 0:D]), (w_q, w_kq_raw[:, :, D:P]))[k]
            sp.dma_start(dst, src.rearrange("(k p) d -> p k d", p=P)).then_inc(consts_loaded, 16)
        sp.dma_start(bias_kq[0:D, :], b_k.rearrange("(d o) -> d o", o=1)).then_inc(consts_loaded, 16)
        sp.dma_start(bias_kq[D:P, :], b_q.rearrange("(d o) -> d o", o=1)).then_inc(consts_loaded, 16)
        sp.dma_start(gam[:, :], gamma.rearrange("(o n) -> o n", o=1).to_broadcast([P, 1])).then_inc(consts_loaded, 16)
        sp.dma_start(bias_out[:, :], b_v.rearrange("(o n) -> o n", o=1).to_broadcast([P, C])).then_inc(consts_loaded, 16)
        sp.dma_start(wv_raw[:, :, :], w_v_in.rearrange("(k p) n -> p k n", p=P)).then_inc(consts_loaded, 16)
        for i, made in enumerate((w_hi_made, w_lo_made)):
            sp.wait_ge(made, 2)
            sp.dma_start(wv_scratch[i], w_v[i][:, :, :].bitcast(FP32).rearrange("p k n -> p (k n)")).then_inc(
                stored[i], 16)
        for i in range(2):
            sp.wait_ge(stored[i], 16)

        def load_xa(n, pair, buf, late):
            if late:
                sp.wait_ge(xt_made[KC - 1], n - 1)
            sp.dma_start(xa[buf][:, :, :], x_tiles[n]).then_inc(xa_loaded[buf], 16)

        for i in range(2):
            load_xa(i, 0, i, False)

        def load_xc(image, at):
            if at.past(2):
                sp.wait_ge(col_mixed[S - 1], at.n - 1)
            sp.dma_start(xc[at.buf][:, :, :], x_cols[image, at.g]).then_inc(xc_loaded[at.buf], 16)

        with sp.Fori(0, B) as image:
            def load_next_xa(at):
                if at.past(2):
                    load_xa(at.n, at.pair, at.buf, True)

            def keep_exps(at):
                sp.wait_ge(row_exps_made, at.n + 1)
                sp.dma_start(e_scratch[at.n], e_rows[at.buf][:, :, :].rearrange("w r l -> w (r l)")).then_inc(
                    row_exps_kept[at.buf], 16)

            def load_first_xc(at):
                if at.known in (2, 3):
                    g = at.known - 2
                    load_xc(image, At(g, image * GC + g, image * (GC // 2), g, g))

            pipeline(sp, image, GR, [(3, load_next_xa), (0, load_first_xc), (-2, keep_exps)])

            pipeline(sp, image, GC, [(2, lambda at: load_xc(image, at) if at.past(2) else None)])

            sp.wait_ge(col_scores_made, (image + 1) * GC)

            def load_wv(at):
                if at.known == 0:
                    for i in range(2):
                        sp.wait_ge(col_mixed[S - 1], (image + 1) * GC - 1 + i)
                        sp.dma_start(w_v[i][:, :, :].bitcast(FP32).rearrange("p k n -> p (k n)"),
                                     wv_scratch[i]).then_inc(wv_loaded, 16)

            def store_out(at):
                sp.wait_ge(out_made[T - 1], at.n + 1)
                sp.dma_start(out_tiles[at.n], xo[at.buf][:, :, :]).then_inc(stored[at.buf], 16)

            def load_xr(at):
                for half in range(2):
                    if at.past(1):
                        sp.wait_ge(row_mixed[half * HALF + HALF - 1], at.n)
                    rows = slice(half * HALF, half * HALF + HALF)
                    sp.dma_start(xr[:, rows, :], x_rows[at.n][:, rows, :]).then_inc(xr_loaded[half], 16)

            def load_exps(at):
                if at.past(2):
                    sp.wait_ge(p_rows_turned, at.n - 1)
                sp.dma_start(e_in[at.buf][:, :, :].rearrange("w r l -> w (r l)"), e_scratch[at.n]).then_inc(
                    e_in_loaded[at.buf], 16)

            def load_xo(at):
                if at.past(2):
                    sp.wait_ge(stored[at.buf], at.pair * 16 + 16)
                sp.dma_start(xo[at.buf][:, :, :], x_tiles[at.n]).then_inc(xo_loaded[at.buf], 16)

            def load_first_xa(at):
                if at.known == GR - 1:
                    following = ((image + 1) % B) * GR
                    for i in range(2):
                        load_xa(following + i, None, i, False)

            pipeline(sp, image, GR, [(-1, store_out), (2, load_xr), (2, load_wv), (4, load_exps), (1, load_xo),
                                     (1, load_first_xa)])
        for i in range(2):
            sp.wait_ge(stored[i], 16 + B * (GR // 2 * 16))
            sp.wait_ge(xa_loaded[i], (B * (GR // 2) + 1) * 16)

    @block.gpsimd
    def _(pool):
        nc.gpsimd.memset(ident[:, :], 0.0)
        nc.gpsimd.memset(diag[:, :], 0.0).then_inc(zeroed, 1)
        pool.wait_ge(zeroed, 1)
        nc.gpsimd.affine_select(out=ident[:, :], in_=ident[:, :], compare_op=ALU.not_equal, fill=1.0, base=0,
                                pattern=[[-1, P]], channel_multiplier=1)
        nc.gpsimd.affine_select(out=diag[:, :], in_=diag[:, :], compare_op=ALU.not_equal, fill=NEG_INF, base=0,
                                pattern=[[-1, L]], channel_multiplier=1).then_inc(consts_made, 1)
        pool.wait_ge(bias_scaled, 1)
        with pool.Fori(0, B) as image:
            def add_bias(at):
                pool.wait_ge(xo_loaded[at.buf], (at.pair + 1) * 16)
                for t in range(T):
                    last = nc.gpsimd.tensor_tensor(xo[at.buf][:, t, :], xo[at.buf][:, t, :], bias_out[:, :], ALU.add)
                last.then_inc(xo_biased, 1)

            pipeline(pool, image, GR, [(0, add_bias)])

    @block.tensor
    def _(pe):
        def turn(dst, src, n):
            return nc.tensor.transpose(dst, src, ident[0:n, 0:n])

        def three_passes(dst, lhs, rhs):
            order = [(k, i, j) for k in range(KC) for i, j in ((0, 0), (0, 1), (1, 0))]
            for k, i, j in order:
                last = nc.tensor.matmul(dst, lhs(i, k), rhs(j, k), start=(k, i, j) == order[0],
                                        stop=(k, i, j) == order[-1])
            return last

        def stay_warm(times):
            for _ in range(times):
                nc.tensor.matmul(bank[B_Z + 1][:, 0:TOK], w_kq[0][:, 0, :],
                                 w_kq[0][:, 0:3, :].rearrange("p k n -> p (k n)"), start=True, stop=True)

        pe.wait_ge(consts_made, 1)
        pe.wait_ge(w_lo_made, 2)
        with pe.Fori(0, B) as image:
            def turn_x(at):
                pe.wait_ge(xa_loaded[at.buf], (at.pair + 1) * 16)
                for k in range(KC):
                    if at.past(1):
                        pe.wait_ge(xt_lo_made[k], at.n)
                    for t in range(T):
                        last = turn(bank[A_XT + k][:, t * P:(t + 1) * P], xa[at.buf][:, t, k * P:(k + 1) * P], P)
                    last.then_inc(xt_made[k], 1)

            def project_kq(at):
                for k in range(KC):
                    pe.wait_ge(xt_lo_made[k], at.n + 1)
                if at.past(2):
                    pe.wait_ge(kq_kept, at.n - 1)
                three_passes(bank[A_KQ + at.buf][:, 0:TOK], lambda i, k: w_kq[i][:, k, :],
                             lambda j, k: (xt_hi, xt_lo)[j][at.buf][:, k, :]).then_inc(kq_made, 1)

            def score_rows(at):
                if at.known == GR - 1:
                    stay_warm(WARM[0])
                pe.wait_ge(kq_kept, at.n + 1)
                pe.wait_ge(q_rows_made, at.n + 1)
                if at.past(2):
                    pe.wait_ge(row_exps_made, at.n - 1)
                for r in range(R):
                    last = nc.tensor.matmul(bank[A_S + at.buf][0:W, r * L:(r + 1) * L],
                                            q_rows[at.buf][:, r * W:(r + 1) * W],
                                            kq[0:D, bass.ds(at.g * TOK + r * W, W)], start=True, stop=True)
                last.then_inc(row_scores_made, 1)

            pipeline(pe, image, GR, [(1, turn_x), (0, project_kq), (-1, score_rows)])

            def turn_stats(at):
                if at.known == 0:
                    pe.wait_ge(row_max_made, (image + 1) * GR)
                    turn(bank[B_NMAX][0:H, 0:W], nmax_row[:, :], W).then_inc(nmax_turned, 1)
                if at.known == 1:
                    pe.wait_ge(row_exps_made, (image + 1) * GR)
                    turn(bank[B_SUM][0:H, 0:W], sum_row[:, :], W).then_inc(sum_turned, 1)

            def score_cols(at):
                if at.known in (0, 1):
                    stay_warm(WARM[1 + at.known])
                pe.wait_ge(q_cols_made, at.n + 1)
                if at.past(2):
                    pe.wait_ge(col_scores_masked, at.n - 1)
                keys = kq[0:D, :].rearrange("d (h w) -> d w h", w=W)
                for s in range(S):
                    last = nc.tensor.matmul(bank[B_S[at.buf]][0:H, s * L:(s + 1) * L], q_cols[at.buf][:, s, :],
                                            keys[:, bass.ds(at.g * S + s, 1), :].rearrange("d o h -> d (o h)"),
                                            start=True, stop=True)
                last.then_inc(col_scores_made, 1)

            def mix_cols(at):
                if at.known in (0, 1):
                    stay_warm(WARM[5 + at.known])
                pe.wait_ge(xc_loaded[at.buf], (at.pair + 1) * 16)
                pe.wait_ge(pt_cols_made, at.n + 1)
                for s in range(S):
                    if at.past(1):
                        pe.wait_ge(col_kept[s], at.n)
                    for k in range(KC):
                        last = nc.tensor.matmul(bank[B_Z + s][:, k * H:(k + 1) * H],
                                                xc[at.buf][:, s, k * P:(k + 1) * P],
                                                pt_cols[:, s * H:(s + 1) * H], start=True, stop=True)
                    last.then_inc(col_mixed[s], 1)

            def turn_p_cols(at):
                if at.known in (0, 1):
                    stay_warm(WARM[3 + at.known])
                if at.known == 0:
                    pe.wait_ge(nmax_t_made, image + 1)
                pe.wait_ge(p_cols_made, at.n + 1)
                if at.past(1):
                    pe.wait_ge(pt_cols_made, at.n)
                for s in range(S):
                    last = turn(bank[B_PT][0:L, s * H:(s + 1) * H], p_cols[at.buf][:, s, :], H)
                last.then_inc(p_cols_turned, 1)

            def turn_factor(at):
                if at.known == GC - 1:
                    pe.wait_ge(factor_made, (image + 1) * GC)
                    turn(bank[B_F][0:W, 0:H], factor[:, :], H).then_inc(factor_turned, 1)

            pipeline(pe, image, GC, [(2, score_cols), (2, turn_stats), (0, mix_cols), (1, turn_p_cols),
                                     (1, turn_factor)])

            def turn_p_rows(at):
                pe.wait_ge(p_rows_made, at.n + 1)
                if at.past(1):
                    pe.wait_ge(pt_rows_made, at.n)
                for r in range(R):
                    last = turn(bank[C_PT][0:L, r * W:(r + 1) * W], e_in[at.buf][:, r, :], W)
                last.then_inc(p_rows_turned, 1)

            def mix_rows(at):
                pe.wait_ge(pt_rows_made, at.n + 1)
                for r in range(R):
                    if at.known == 0 and r < S:
                        pe.wait_ge(col_kept[r], (image + 1) * GC)
                    if r % HALF == 0:
                        pe.wait_ge(xr_loaded[r // HALF], (at.n + 1) * 16)
                    if at.past(1):
                        pe.wait_ge(row_added[r], at.n)
                    for k in range(KC):
                        last = nc.tensor.matmul(bank[C_Z + r][:, k * W:(k + 1) * W], xr[:, r, k * P:(k + 1) * P],
                                                pt_rows[:, r * W:(r + 1) * W], start=True, stop=True)
                    last.then_inc(row_mixed[r], 1)

            def project_v(at):
                if at.known == 0:
                    pe.wait_ge(wv_loaded, (image + 1) * 32)
                for t in range(T):
                    slot = (at.buf + t) % 2
                    pe.wait_ge(mix_lo_made[t], at.n + 1)
                    if at.past(1):
                        pe.wait_ge(out_made[t], at.n)
                    three_passes(bank[C_Y + t][:, :], lambda i, k: (mix_hi, mix_lo)[i][slot][:, k, :],
                                 lambda j, k: w_v[j][:, k, :]).then_inc(projected[t], 1)

            pipeline(pe, image, GR, [(1, mix_rows), (2, turn_p_rows), (0, project_v)])
            for t in range(T):
                pe.wait_ge(out_made[t], (image + 1) * GR)

    @block.scalar
    def _(act):
        act.wait_ge(consts_loaded, 7 * 16)
        nc.scalar.copy(w_kq[0][:, :, :], w_kq_raw[:, :, :]).then_inc(w_hi_made, 1)
        act.wait_ge(wv_scaled, 1)
        nc.scalar.copy(w_v[0][:, :, :], wv_raw[:, :, :]).then_inc(w_hi_made, 1)
        with act.Fori(0, B) as image:
            def exp_rows(at):
                act.wait_ge(row_max_made, at.n + 1)
                if at.past(2):
                    act.wait_ge(row_exps_kept[at.buf], at.pair * 16)
                for r in range(R):
                    row = at.g * R + r
                    last = nc.scalar.activation(e_rows[at.buf][:, r, :], bank[A_S + at.buf][0:W, r * L:(r + 1) * L],
                                                ACT.Exp, bias=nmax_row[:, bass.ds(row, 1)],
                                                accum_out=sum_row[:, bass.ds(row, 1)])
                last.then_inc(row_exps_made, 1)

            def split_xt(at):
                if at.past(2):
                    act.wait_ge(kq_made, at.n - 1)
                for k in range(KC):
                    act.wait_ge(xt_made[k], at.n + 1)
                    nc.scalar.copy(xt_hi[at.buf][:, k, :], bank[A_XT + k][:, 0:TOK]).then_inc(xt_hi_made[k], 1)

            def keep_kq(at):
                if at.known == 3:
                    for i in range(2):
                        act.wait_ge(stored[i], image * (GR // 2 * 16) + 16)
                act.wait_ge(kq_made, at.n + 1)
                nc.scalar.activation(kq[:, bass.ds(at.g * TOK, TOK)].rearrange("d (p t) -> d t p", t=T),
                                     bank[A_KQ + at.buf][:, 0:TOK].rearrange("d (t p) -> d t p", t=T),
                                     ACT.Identity, bias=bias_kq[:, :]).then_inc(kq_kept, 1)

            pipeline(act, image, GR, [(1, split_xt), (-2, exp_rows), (0, keep_kq)])

            def keep_col(at, s):
                if at.known == 0 and s == 0:
                    for i in range(2):
                        act.wait_ge(row_exps_kept[i], (image + 1) * (GR // 2 * 16))
                act.wait_ge(col_mixed[s], at.n + 1)
                to = mixed[:, :, :].rearrange("c k (h w) -> c w k h", w=W)
                nc.scalar.copy(to[:, bass.ds(at.g * S + s, 1), :, :].rearrange("c o k h -> c (o k) h"),
                               bank[B_Z + s][:, 0:KC * H].rearrange("c (k h) -> c k h", k=KC)).then_inc(col_kept[s], 1)

            def exp_cols(at):
                act.wait_ge(joint_max_made, at.n + 1)
                for s in range(S):
                    nc.scalar.activation(p_cols[at.buf][:, s, :], p_cols[at.buf][:, s, :], ACT.Exp,
                                         bias=nmax[at.buf][:, s:s + 1], accum_out=sum_col[at.buf][:, s:s + 1])
                act.wait_ge(gap_made, at.n + 1)
                nc.scalar.activation(shrink[at.buf][:, :], gap[at.buf][:, :], ACT.Exp).then_inc(shrink_made, 1)

            def keep_pt_cols(at):
                act.wait_ge(p_cols_turned, at.n + 1)
                if at.past(1):
                    act.wait_ge(col_mixed[S - 1], at.n)
                nc.scalar.copy(pt_cols[:, :], bank[B_PT][0:L, 0:S * H]).then_inc(pt_cols_made, 1)

            pipeline(act, image, GC, [(1, exp_cols), (0, lambda at: keep_col(at, 0)), (0, lambda at: keep_col(at, 1)),
                                      (0, lambda at: keep_col(at, 2)), (1, keep_pt_cols)])

            def keep_pt_rows(at):
                act.wait_ge(p_rows_turned, at.n + 1)
                if at.past(1):
                    act.wait_ge(row_mixed[R - 1], at.n)
                nc.scalar.copy(pt_rows[:, :], bank[C_PT][0:L, 0:R * W]).then_inc(pt_rows_made, 1)

            def split_mix(at, t):
                act.wait_ge(row_added[R - 1], at.n + 1)
                if t >= 2:
                    act.wait_ge(projected[t - 2], at.n + 1)
                elif at.past(1):
                    act.wait_ge(projected[t + T - 2], at.n)
                tokens = mixed[:, :, bass.ds(at.g * TOK, TOK)].rearrange("c k (p t) -> c t k p", t=T)
                nc.scalar.copy(mix_hi[(at.buf + t) % 2][:, :, :], tokens[:, t, :, :]).then_inc(mix_hi_made[t], 1)

            pipeline(act, image, GR, [(0, lambda at: split_mix(at, 1)), (2, keep_pt_rows),
                                      (0, lambda at: split_mix(at, 2)), (1, lambda at: split_mix(at, 0))])

    @block.vector
    def _(dve):
        dve.wait_ge(consts_loaded, 7 * 16)
        nc.vector.tensor_scalar(bias_out[:, :], bias_out[:, :], gam[:, :], None, ALU.mult).then_inc(bias_scaled, 1)
        nc.vector.tensor_scalar(wv_raw[:, :, :], wv_raw[:, :, :], gam[:, :], None, ALU.mult).then_inc(wv_scaled, 1)
        dve.wait_ge(w_hi_made, 1)
        nc.vector.tensor_tensor(w_kq[1][:, :, :], w_kq_raw[:, :, :], w_kq[0][:, :, :].bitcast(FP32),
                                ALU.subtract).then_inc(w_lo_made, 1)
        dve.wait_ge(w_hi_made, 2)
        dve.wait_ge(wv_scaled, 1)
        nc.vector.tensor_tensor(w_v[1][:, :, :], wv_raw[:, :, :], w_v[0][:, :, :].bitcast(FP32),
                                ALU.subtract).then_inc(w_lo_made, 1)
        for i in range(2):
            dve.wait_ge(stored[i], 16)
        with dve.Fori(0, B) as image:
            def max_rows(at):
                dve.wait_ge(row_scores_made, at.n + 1)
                nc.vector.tensor_reduce(nmax_row[:, bass.ds(at.g * R, R)],
                                        bank[A_S + at.buf][0:W, 0:R * L].rearrange("w (r l) -> w r l", r=R),
                                        axis=AX.X, op=ALU.max, negate=True).then_inc(row_max_made, 1)

            def split_xt(at):
                for k in range(KC):
                    dve.wait_ge(xt_hi_made[k], at.n + 1)
                    nc.vector.tensor_tensor(xt_lo[at.buf][:, k, :], bank[A_XT + k][:, 0:TOK],
                                            xt_hi[at.buf][:, k, :].bitcast(FP32), ALU.subtract).then_inc(xt_lo_made[k], 1)

            def keep_q_rows(at):
                dve.wait_ge(kq_kept, at.n + 1)
                if at.past(2):
                    dve.wait_ge(row_scores_made, at.n - 1)
                nc.vector.tensor_copy(q_rows[at.buf][:, :], kq[D:P, bass.ds(at.g * TOK, TOK)]).then_inc(q_rows_made, 1)

            def keep_q_cols(at):
                if at.past(2):
                    dve.wait_ge(col_scores_made, at.n - 1)
                nc.vector.tensor_copy(q_cols[at.buf][:, :, :], kq[D:P, :].rearrange("d (h w) -> d w h", w=W)[
                    :, bass.ds(at.g * S, S), :]).then_inc(q_cols_made, 1)

            def keep_first_q_cols(at):
                if at.known == GR - 1:
                    for g in range(2):
                        keep_q_cols(At(g, image * GC + g, image * (GC // 2), g, g))

            pipeline(dve, image, GR, [(-2, max_rows), (1, split_xt), (0, keep_q_rows), (0, keep_first_q_cols)])


            def max_cols(at):
                dve.wait_ge(col_scores_made, at.n + 1)
                if at.past(2):
                    dve.wait_ge(p_cols_turned, at.n - 1)
                p = p_cols[at.buf]
                nc.vector.tensor_tensor(p[:, :, :], bank[B_S[at.buf]][0:H, 0:S * L].rearrange("h (s l) -> h s l", s=S),
                                        diag[:, :].unsqueeze(1).to_broadcast([H, S, L]),
                                        ALU.add).then_inc(col_scores_masked, 1)
                dve.wait_ge(col_scores_masked, at.n + 1)
                nc.vector.tensor_reduce(nmax_col[at.buf][:, :], p[:, :, :], axis=AX.X, op=ALU.max,
                                        negate=True).then_inc(col_max_made, 1)
                if at.known == 0:
                    dve.wait_ge(nmax_turned, image + 1)
                    nc.vector.tensor_copy(nmax_row_t[:, :], bank[B_NMAX][0:H, 0:W]).then_inc(nmax_t_made, 1)
                    dve.wait_ge(nmax_t_made, image + 1)
                cols = bass.ds(at.g * S, S)
                dve.wait_ge(col_max_made, at.n + 1)
                nc.vector.tensor_tensor(nmax[at.buf][:, :], nmax_col[at.buf][:, :], nmax_row_t[:, cols],
                                        ALU.min).then_inc(joint_max_made, 1)
                dve.wait_ge(joint_max_made, at.n + 1)
                nc.vector.tensor_tensor(gap[at.buf][:, :], nmax[at.buf][:, :], nmax_row_t[:, cols],
                                        ALU.subtract).then_inc(gap_made, 1)

            def normalise_cols(at):
                cols = bass.ds(at.g * S, S)
                u = at.buf
                if at.known == 0:
                    dve.wait_ge(sum_turned, image + 1)
                    nc.vector.tensor_copy(sum_row_t[:, :], bank[B_SUM][0:H, 0:W]).then_inc(sum_t_made, 1)
                    dve.wait_ge(sum_t_made, image + 1)
                dve.wait_ge(shrink_made, at.n + 1)
                nc.vector.tensor_tensor(row_part[u][:, :], shrink[u][:, :], sum_row_t[:, cols],
                                        ALU.mult).then_inc(row_part_made, 1)
                dve.wait_ge(row_part_made, at.n + 1)
                nc.vector.tensor_tensor(total[u][:, :], row_part[u][:, :], sum_col[u][:, :],
                                        ALU.add).then_inc(total_made, 1)
                dve.wait_ge(total_made, at.n + 1)
                nc.vector.reciprocal(inv[u][:, :], total[u][:, :]).then_inc(inv_made, 1)
                dve.wait_ge(inv_made, at.n + 1)
                nc.vector.tensor_tensor(p_cols[u][:, :, :], p_cols[u][:, :, :],
                                        inv[u][:, :].unsqueeze(2).to_broadcast([H, S, L]),
                                        ALU.mult).then_inc(p_cols_made, 1)
                nc.vector.tensor_tensor(factor[:, cols], shrink[u][:, :], inv[u][:, :],
                                        ALU.mult).then_inc(factor_made, 1)

            pipeline(dve, image, GC, [(3, lambda at: keep_q_cols(at) if at.past(2) else None), (2, max_cols),
                                      (1, normalise_cols)])

            dve.wait_ge(factor_turned, image + 1)
            nc.vector.tensor_copy(factor_t[:, :], bank[B_F][0:W, 0:H]).then_inc(factor_t_made, 1)
            dve.wait_ge(factor_t_made, image + 1)
            for s in range(S):
                dve.wait_ge(col_kept[s], (image + 1) * GC)

            def normalise_rows(at):
                dve.wait_ge(e_in_loaded[at.buf], (at.pair + 1) * 16)
                e = e_in[at.buf]
                nc.vector.tensor_tensor(e[:, :, :], e[:, :, :],
                                        factor_t[:, bass.ds(at.g * R, R)].unsqueeze(2).to_broadcast([W, R, L]),
                                        ALU.mult).then_inc(p_rows_made, 1)

            def add_rows(at):
                for r in range(R):
                    dve.wait_ge(row_mixed[r], at.n + 1)
                    tokens = mixed[:, :, bass.ds(at.g * TOK + r * W, W)]
                    nc.vector.tensor_tensor(tokens, bank[C_Z + r][:, 0:KC * W].rearrange("c (k w) -> c k w", k=KC),
                                            tokens, ALU.add).then_inc(row_added[r], 1)

            def split_mix(at, t):
                dve.wait_ge(mix_hi_made[t], at.n + 1)
                slot = (at.buf + t) % 2
                tokens = mixed[:, :, bass.ds(at.g * TOK, TOK)].rearrange("c k (p t) -> c t k p", t=T)
                nc.vector.tensor_tensor(mix_lo[slot][:, :, :], tokens[:, t, :, :],
                                        mix_hi[slot][:, :, :].bitcast(FP32), ALU.subtract).then_inc(mix_lo_made[t], 1)

            def finish(at, t):
                dve.wait_ge(projected[t], at.n + 1)
                dve.wait_ge(xo_biased, at.n + 1)
                nc.vector.tensor_tensor(xo[at.buf][:, t, :], bank[C_Y + t][:, :], xo[at.buf][:, t, :],
                                        ALU.add).then_inc(out_made[t], 1)

            pipeline(dve, image, GR, [(-1, lambda at: finish(at, 2)), (2, normalise_rows), (1, add_rows),
                                      (0, lambda at: split_mix(at, 1)), (0, lambda at: finish(at, 0)),
                                      (0, lambda at: split_mix(at, 2)), (0, lambda at: finish(at, 1)),
                                      (1, lambda at: split_mix(at, 0))])

    ctx.close()


_INS = ["x", "L0_conv_Wq", "L0_conv_bq", "L0_conv_Wk", "L0_conv_bk", "L0_conv_Wv", "L0_conv_bv", "L0_conv_gamma"]


def kernel(**inputs):
    import numpy as _np
    import concourse.bacc as _bacc
    from concourse import mybir as _mybir
    from concourse.bass_utils import run_bass_kernel_spmd as _run

    nc = _bacc.Bacc("TRN2", target_bir_lowering=False, num_devices=1)
    arrays, args = {}, []
    for name in _INS:
        a = _np.ascontiguousarray(inputs[name])
        if a.ndim == 0:
            a = a.reshape(1)
        arrays[f"in_{name}"] = a
        args.append(nc.dram_tensor(f"in_{name}", a.shape, _mybir.dt.from_np(a.dtype), kind="ExternalInput").ap())
    out = nc.dram_tensor("out", inputs["x"].shape, _mybir.dt.float32, kind="ExternalOutput").ap()
    criss_cross_attention(nc, *args, out)
    r = _run(nc, [arrays], core_ids=[0])
    return r.results[0]["out"]
```
